# Optimizing a Trainium2 kernel written in Bass

```python
import numpy as np
import jax
import jax.numpy as jnp

def _softmax(x, axis=-1):
    return jax.nn.softmax(x, axis=axis)

def _gelu(x):
    return jax.nn.gelu(x, approximate=True)

def _silu(x):
    return jax.nn.silu(x)

def _sigmoid(x):
    return jax.nn.sigmoid(x)

def _layernorm(x, axis=-1, eps=1e-05):
    m = jnp.mean(x, axis=axis, keepdims=True)
    v = jnp.var(x, axis=axis, keepdims=True)
    return (x - m) / jnp.sqrt(v + eps)

def _scatter_add(tgt, idx, src, axis=0):
    return tgt.at[idx].add(src)

def _segment_sum(src, seg, n):
    return jax.ops.segment_sum(src, seg, n)
kernel_name = 'mk_rec_standalone_d1_rec_r8_79e6eb'

def setup_inputs(seed: int=0):
    np.random.seed(seed)
    _w = jnp.asarray

    def _rec_inputs():
        import jax
        import jax.numpy as jnp
        _rk = jax.random.key(seed)
        r_x = jax.random.randint(jax.random.fold_in(_rk, 1), (1024, 32), 0, 1000, jnp.int32)
        return r_x
    r_x = _rec_inputs()

    def _L0_rec_setup():
        import jax, jax.numpy as jnp
        import numpy as np
        F = 32
        V = 1000
        D = 64
        B = 1024
        P = F * (F - 1) // 2
        IN = F * D + P
        H1, H2, OUT = (1024, 512, 1000)
        key = jax.random.key(seed)
        ks = jax.random.split(key, 8)
        x = jax.random.randint(ks[0], (B, F), 0, V)
        emb_tables = jax.random.normal(ks[1], (F, V, D), dtype=jnp.float32) * 0.05
        W1 = jax.random.normal(ks[2], (IN, H1), dtype=jnp.float32) * (1.0 / np.sqrt(IN))
        b1 = jnp.zeros((H1,), dtype=jnp.float32)
        W2 = jax.random.normal(ks[3], (H1, H2), dtype=jnp.float32) * (1.0 / np.sqrt(H1))
        b2 = jnp.zeros((H2,), dtype=jnp.float32)
        W3 = jax.random.normal(ks[4], (H2, OUT), dtype=jnp.float32) * (1.0 / np.sqrt(H2))
        b3 = jnp.zeros((OUT,), dtype=jnp.float32)
        return {'x': x, 'emb_tables': emb_tables, 'W1': W1, 'b1': b1, 'W2': W2, 'b2': b2, 'W3': W3, 'b3': b3}
    _L0_rec_all = _L0_rec_setup()
    _L0_rec_in = {k: v for k, v in _L0_rec_all.items() if k in ('emb_tables', 'W1', 'b1', 'W2', 'b2', 'W3', 'b3')}
    del _L0_rec_all
    return {'r_x': r_x, 'L0_rec_emb_tables': _L0_rec_in['emb_tables'], 'L0_rec_W1': _L0_rec_in['W1'], 'L0_rec_b1': _L0_rec_in['b1'], 'L0_rec_W2': _L0_rec_in['W2'], 'L0_rec_b2': _L0_rec_in['b2'], 'L0_rec_W3': _L0_rec_in['W3'], 'L0_rec_b3': _L0_rec_in['b3']}

def reference(r_x, L0_rec_emb_tables, L0_rec_W1, L0_rec_b1, L0_rec_W2, L0_rec_b2, L0_rec_W3, L0_rec_b3):
    import jax
    import jax.numpy as jnp

    def _L0_rec_ref(x, emb_tables, W1, b1, W2, b2, W3, b3):
        import jax, jax.numpy as jnp
        import numpy as np
        F = 32
        V = 1000
        D = 64
        B = 1024
        P = F * (F - 1) // 2
        IN = F * D + P
        H1, H2, OUT = (1024, 512, 1000)
        e = emb_tables[jnp.arange(F)[None, :], x]
        gram = jnp.einsum('bid,bjd->bij', e, e)
        iu, ju = jnp.triu_indices(F, k=1)
        cross = gram[:, iu, ju]
        h = jnp.concatenate([e.reshape(B, F * D), cross], axis=1)
        h = jax.nn.relu(h @ W1 + b1)
        h = jax.nn.relu(h @ W2 + b2)
        logits = h @ W3 + b3
        return jax.nn.sigmoid(logits)
    y = _L0_rec_ref(r_x, L0_rec_emb_tables, L0_rec_W1, L0_rec_b1, L0_rec_W2, L0_rec_b2, L0_rec_W3, L0_rec_b3)
    return y

_drawn_inputs = setup_inputs


def setup_inputs(seed=0):
    import zlib

    import numpy as np

    out = dict(_drawn_inputs(seed))
    spreads = {'L0_rec_b1': (0.0, 0.384), 'L0_rec_b2': (0.0, 0.312), 'L0_rec_b3': (0.0, 0.1)}
    factors = {'L0_rec_emb_tables': 5.513, 'L0_rec_W1': 5.502}
    for name, (base, spread) in spreads.items():
        noise = np.random.default_rng([zlib.crc32(name.encode()), seed]).standard_normal(out[name].shape)
        drawn = base * np.exp(spread * noise) if base else spread * noise
        out[name] = jnp.asarray(drawn.astype(out[name].dtype))
    for name, factor in factors.items():
        out[name] = (out[name] * factor).astype(out[name].dtype)
    return out
```

```python
import concourse.bass as bass
from concourse import mybir
from contextlib import ExitStack

P = 128
B, F, V, D = 1024, 32, 1000, 64
H1, H2, OUT = 1024, 512, 1000
NB = 256
BLOCKS = B // NB
BT = NB // P
KT = F * D // P
QB = NB // 4
GJ = QB // 4
CROSS = 4
GROW = F + F // 2
OT = 125
RESIDENT = 8
RAWS = 4
RING = 4
XRING = 8


def recsys_kernel(nc, x, tables, w1, b1, w2, b2, w3, b3, ident_in, out):
    fp32, fp32r, i32 = mybir.dt.float32, mybir.dt.float32r, mybir.dt.int32
    ALU = mybir.AluOpType
    ACT = mybir.ActivationFunctionType

    EMB = [("emb", k) for k in range(KT)]
    L2 = [("l2", k) for k in range(4)]
    PAIR = [("pair", k) for k in range(CROSS)]
    L3 = [("l3", k) for k in range(4)]
    FIRST, BODY, LAST = EMB + PAIR, EMB + L2 + PAIR + L3, L2 + L3
    GRAM_AFTER = KT - 5
    AHEAD = {k: [k + 2] for k in range(6)} | {6: [8, 9], 7: [10, 11], 8: [12, 13], 9: [14], 10: [15]}

    def tiles_ahead(steps, after, u):
        kind, k = steps[u]
        own = [(0, j) for j in AHEAD.get(k, [])] if kind == "emb" else []
        return own + [(1, u + 2 - len(steps))] * (u + 2 >= len(steps) and after[:1] == EMB[:1])

    def first_seq(n):
        return len(BODY) * n + (len(FIRST) - len(BODY))

    def streamed(steps):
        return [s for s in steps if not (s[0] == "emb" and s[1] < RESIDENT)]

    assert len(FIRST) % RING == 0 and len(BODY) % RING == 0
    assert len(streamed(FIRST)) % RAWS == 0 and len(streamed(BODY)) % RAWS == 0

    def is_start(base):
        return isinstance(base, int) and base == 0

    def raw_uses(n):
        per_body, per_first = (len(streamed(x)) // RAWS for x in (BODY, FIRST))
        return per_body * n + (per_first - per_body)

    gd = nc.dram_tensor("gram_scratch", [4 * F, GROW, QB], fp32, kind="Internal").ap()

    ctx = ExitStack()
    with ctx:
        def sb(name, shape, dt):
            return ctx.enter_context(nc.sbuf_tensor(name, shape, dt))

        def pb(name, shape, dt):
            return ctx.enter_context(nc.psum_tensor(name, shape, dt))

        def sem(name):
            return ctx.enter_context(nc.semaphore(name))

        xi = sb("xi", [P, BLOCKS, BT, F], i32)
        offs = sb("offs", [P, BT, F], i32)
        idx = sb("idx", [P, BT, F], i32)
        ident = sb("ident", [P, P], fp32)
        b1s = sb("b1s", [P, H1 // P], fp32)
        b2s = sb("b2s", [P, H2 // P], fp32)
        b3s = sb("b3s", [OT, OUT // OT], fp32)
        emb = sb("emb", [P, KT, BT, 2 * D], fp32)
        xhi = sb("xhi", [P, XRING, NB], fp32r)
        xlo = sb("xlo", [P, XRING, NB], fp32r)
        z = sb("z", [P, QB, 4, F], fp32)
        dg = sb("dg", [P, F, QB], fp32)
        gc = sb("gc", [P, 4, CROSS, QB], fp32)
        gchi = sb("gchi", [P, CROSS, NB], fp32r)
        gclo = sb("gclo", [P, CROSS, NB], fp32r)
        h1hi = sb("h1hi", [P, H1 // P, NB], fp32r)
        h1lo = sb("h1lo", [P, H1 // P, NB], fp32r)
        h2hi = sb("h2hi", [P, H2 // P, NB], fp32r)
        h2lo = sb("h2lo", [P, H2 // P, NB], fp32r)
        res = sb("res", [OT, 2, 2 * NB], fp32)
        wres = sb("wres", [P, RESIDENT, H1], fp32)
        wraw = sb("wraw", [P, RAWS, H1], fp32)
        whi = sb("whi", [P, RING, H1], fp32r)
        wlo = sb("wlo", [P, RING, H1], fp32r)

        h1p = pb("h1p", [P, 4, 512], fp32)
        misc = pb("misc", [P, 4, 512], fp32)
        tgp = misc[:, 0:2, :]
        l2p = misc[:, 2:4, :]

        s_const = sem("s_const")
        s_x = sem("s_x")
        s_offs = sem("s_offs")
        s_idx = sem("s_idx")
        s_slot = sem("s_slot")
        s_emb = [sem(f"s_emb{k}") for k in range(KT)]
        s_first = [sem(f"s_first{k}") for k in range(KT)]
        s_early = sem("s_early")
        s_zeven = sem("s_zeven")
        s_zodd = sem("s_zodd")
        s_res = [sem(f"s_res{k}") for k in range(RESIDENT)]
        s_raw = [sem(f"s_raw{k}") for k in range(RAWS)]
        s_whi = sem("s_whi")
        s_wlo = sem("s_wlo")
        s_used = sem("s_used")
        s_t = sem("s_t")
        s_xhi = sem("s_xhi")
        s_xlo = sem("s_xlo")
        s_gram = sem("s_gram")
        s_dga = sem("s_dga")
        s_dgv = sem("s_dgv")
        s_gdw = sem("s_gdw")
        s_gc = sem("s_gc")
        s_gchi = sem("s_gchi")
        s_gclo = sem("s_gclo")
        s_h1r = sem("s_h1r")
        s_h1hi = sem("s_h1hi")
        s_h1lo = sem("s_h1lo")
        s_h2r = sem("s_h2r")
        s_h2hi = sem("s_h2hi")
        s_h2lo = sem("s_h2lo")
        s_sig = sem("s_sig")
        s_out = [sem(f"s_out{k}") for k in range(2)]

        block = ctx.enter_context(nc.Block())

        def by_sample(cols):
            return cols.rearrange("p (t c q) -> p t c q", c=4, q=P // 4)

        def in_order(cols):
            return cols.rearrange("p (c t q) -> p t c q", t=BT, q=P // 4)

        def z_of(f, tiles):
            return z[0:D, P // 4 * tiles.start:P // 4 * tiles.stop, :, f].rearrange(
                "d (t q) c -> d t c q", q=P // 4)

        def tiles_left(n):
            return slice(1, BT) if isinstance(n, int) and n == 0 else slice(0, BT)

        def raw_chunk(kind, k, r):
            if kind == "emb" and k < RESIDENT:
                return wres[:, k, :]
            return wraw[:, r % RAWS, 0:OUT if kind == "l3" else H1]

        def chunk_in_dram(kind, k):
            if kind == "emb":
                return w1[k]
            if kind == "pair":
                return w1[KT + k]
            return w2[k] if kind == "l2" else w3[k]

        @block.sync
        def _(sp):
            sp.dma_start(xi[:], x).then_inc(s_x, 16)
            sp.dma_start(ident[:], ident_in).then_inc(s_const, 16)
            sp.dma_start(b1s[:], b1).then_inc(s_const, 16)
            sp.dma_start(b2s[:], b2).then_inc(s_const, 16)
            sp.dma_start(b3s[:], b3).then_inc(s_const, 16)
            for k in range(RESIDENT):
                if k >= 3:
                    sp.wait_ge(s_first[k - 3], 32)
                sp.dma_start(wres[:, k, :], w1[k]).then_inc(s_res[k], 16)

            def stream(steps, which, base):
                at = [u for u, step in enumerate(steps) if step in streamed(steps)]
                for r in which:
                    kind, k = steps[at[r]]
                    if r >= RAWS:
                        sp.wait_ge(s_wlo, base + at[r - RAWS] + 1)
                    elif not is_start(base):
                        sp.wait_ge(s_wlo, base - RAWS + r + 1)
                    else:
                        sp.wait_ge(s_first[k - 3], 32)
                    sp.dma_start(wraw[:, r % RAWS, 0:OUT if kind == "l3" else H1],
                                 chunk_in_dram(kind, k)).then_inc(s_raw[r % RAWS], 16)

            def relocate(n):
                sp.wait_ge(s_dga, GJ // 2 * n + GJ // 2)
                sp.wait_ge(s_dgv, GJ // 2 * n + GJ // 2)
                sp.dma_start(gd[:, 0:F, :], dg[:]).then_inc(s_gdw, 16)
                sp.dma_start(gd[:, F:GROW, :], dg[:, 0:F // 2, :]).then_inc(s_gdw, 16)
                sp.wait_ge(s_gdw, 32 * n + 32)
                for kk in range(4):
                    src = bass.AP(tensor=gd.tensor, offset=(CROSS * kk + 1) * QB,
                                  ap=[[(GROW + 1) * QB, F], [F * GROW * QB, 4], [1, CROSS * QB]])
                    sp.dma_start(gc[F * kk:F * (kk + 1), :, :, :].rearrange("i c t q -> i c (t q)"),
                                 src).then_inc(s_gc, 16)

            def loads(steps, n):
                base = 0 if isinstance(n, int) and n == 0 else first_seq(n)
                at = [u for u, step in enumerate(steps) if step in streamed(steps)]
                early = sum(r < RAWS or at[r - RAWS] <= GRAM_AFTER + 2 for r in range(len(at)))
                stream(steps, range(early), base)
                if not is_start(base):
                    sp.wait_ge(s_gclo, n)
                relocate(n)
                stream(steps, range(early, len(at)), base)

            loads(FIRST, 0)
            with sp.Fori(1, BLOCKS - 1) as n:
                loads(BODY, n)
            loads(BODY, BLOCKS - 1)
            stream(LAST, range(len(LAST)), first_seq(BLOCKS))

        @block.gpsimd
        def _(pool):
            nc.gpsimd.iota(offs[:], [[0, BT], [V, F]], base=0, channel_multiplier=0).then_inc(s_offs, 1)
            pool.wait_ge(s_x, 16)
            pool.wait_ge(s_offs, 1)

            def gather(k, t, landed):
                for f in range(2):
                    nc.gpsimd.indirect_dma_start(
                        emb[:, k, t, f * D:(f + 1) * D], None, tables,
                        bass.IndirectOffsetOnAxis(ap=idx[:, t, 2 * k + f:2 * k + f + 1], axis=0),
                    ).then_inc(landed, 16)

            nc.gpsimd.tensor_tensor(idx[:], xi[:, 0], offs[:], ALU.add).then_inc(s_idx, 1)
            pool.wait_ge(s_idx, 1)
            for t, landed in enumerate((s_first, s_emb)):
                for k in range(KT):
                    gather(k, t, landed[k])
            for k in range(KT):
                pool.wait_ge(s_first[k], 32)
            with pool.Fori(1, BLOCKS) as n:
                for k in range(KT):
                    pool.wait_ge(s_emb[k], 32 * BT * n - 32)
                nc.gpsimd.tensor_tensor(idx[:], xi[:, bass.ds(n, 1)].rearrange("p n t f -> p (n t) f"),
                                        offs[:], ALU.add).then_inc(s_idx, 1)
                pool.wait_ge(s_idx, n + 1)
                pool.sem_inc(s_slot, 1)
                for k in range(KT):
                    pool.wait_ge(s_t, KT * (n - 1) + k + 1)
                    pool.sem_inc(s_slot, 1)
                    for t in range(BT):
                        gather(k, t, s_emb[k])

        @block.scalar
        def _(act):
            act.wait_ge(s_const, 64)
            for j in range(2):
                act.sem_inc(s_out[j], 16)

            def weight_hi(steps, u, base, used):
                if u >= len(steps):
                    return
                kind, k = steps[u]
                r = sum(step in streamed(steps) for step in steps[:u])
                if kind == "emb" and k < RESIDENT:
                    act.wait_ge(s_res[k], 16)
                else:
                    act.wait_ge(s_raw[r % RAWS], 16 * (used + r // RAWS + 1))
                if u >= RING or not is_start(base):
                    act.wait_ge(s_used, base + u - RING + 1)
                src = raw_chunk(kind, k, r)
                nc.scalar.copy(whi[:, u % RING, 0:src.shape[1]], src).then_inc(s_whi, 1)

            def even_to_z(k, tiles):
                cols = slice(P * tiles.start, P * tiles.stop)
                return nc.scalar.copy(z_of(2 * k, tiles), by_sample(tgp[0:D, k % 2, cols]))

            def embedding_hi(n, k):
                act.wait_ge(s_t, KT * n + k + 1)
                nc.scalar.copy(in_order(xhi[:, k % XRING, :]), by_sample(tgp[:, k % 2, 0:NB]))
                even_to_z(k, tiles_left(n)).then_inc(s_xhi, 1)

            def gram_copies(n, jobs):
                for g in jobs:
                    act.wait_ge(s_gram, GJ * n + g + 1)
                    for c in range(4):
                        last = nc.scalar.copy(
                            dg[F * c:F * (c + 1), :, 4 * g:4 * g + 4].rearrange("p j q -> p q j"),
                            misc[F * c:F * (c + 1), g % 4, :].rearrange(
                                "p (q j) -> p q j", q=4)[:, :, F * c:F * (c + 1)])
                    last.then_inc(s_dga, 1)

            def pairs_hi(n):
                act.wait_ge(s_gc, 64 * n + 64)
                nc.scalar.copy(gchi[:].rearrange("p t (c q) -> p c t q", c=4), gc[:]).then_inc(s_gchi, 1)

            def layer_hi(n, banks, src, dst, relued, written, per_block):
                for j in banks:
                    act.wait_ge(relued, per_block * n + j + 1)
                    nc.scalar.copy(dst[:, 2 * j:2 * j + 2, :],
                                   src[:, j, :].rearrange("p (i b) -> p i b", i=2)).then_inc(written, 1)

            def outputs(m, j, done):
                act.wait_ge(s_used, done)
                act.wait_ge(s_out[j % 2], 32 * m + 16 * (j // 2 + 1))
                for i in range(2):
                    last = nc.scalar.activation(res[:, j % 2, NB * i:NB * (i + 1)],
                                                l2p[0:OT, j % 2, NB * i:NB * (i + 1)], ACT.Sigmoid,
                                                bias=b3s[:, 2 * j + i:2 * j + i + 1])
                last.then_inc(s_sig, 1)
                act.wait_ge(s_sig, 4 * m + j + 1)
                act.dma_start(out.rearrange("(t p) b -> p t b", p=OT)[:, 2 * j:2 * j + 2, bass.ds(m * NB, NB)],
                              res[:, j % 2, :].rearrange("p (i b) -> p i b", i=2)).then_inc(s_out[j % 2], 16)

            def run(steps, after, n, m, base, used):
                if is_start(base):
                    for u in range(3):
                        weight_hi(steps, u, base, used)
                    for k in range(KT):
                        act.wait_ge(s_early, k + 1)
                        even_to_z(k, slice(0, 1)).then_inc(s_zeven, 1)
                    gram_copies(n, range(0, GJ // 2, 2))
                    embedding_hi(n, 0)
                    embedding_hi(n, 1)
                for u, (kind, k) in enumerate(steps):
                    for i, j in tiles_ahead(steps, after, u):
                        embedding_hi(n + i, j)
                    weight_hi(steps + after, u + 3, base, used)
                    if kind == "emb" and k == GRAM_AFTER - 1:
                        if is_start(base):
                            gram_copies(n, range(GJ // 2, GJ, 2))
                        else:
                            act.wait_ge(s_gdw, 32 * n)
                            gram_copies(n, range(0, GJ, 2))
                    if kind == "l2" and k == 1:
                        layer_hi(m, [0], l2p, h2hi, s_h2r, s_h2hi, 2)
                    if kind == "l2" and k == 3:
                        layer_hi(m, [1], l2p, h2hi, s_h2r, s_h2hi, 2)
                    if (kind, k) in (("l2", 2), ("emb", KT - 1)) and n is not None and (
                            kind == "l2" or len(steps) == len(FIRST)):
                        pairs_hi(n)
                    if kind == "pair" and k == CROSS - 1:
                        layer_hi(n, range(4), h1p, h1hi, s_h1r, s_h1hi, 4)
                    if kind == "l3":
                        outputs(m, k, base + u + 1)

            run(FIRST, BODY, 0, None, 0, 0)
            with act.Fori(1, BLOCKS - 1) as n:
                run(BODY, BODY, n, n - 1, first_seq(n), raw_uses(n))
            n = BLOCKS - 1
            run(BODY, LAST, n, n - 1, first_seq(n), raw_uses(n))
            run(LAST, [], None, n, first_seq(BLOCKS), raw_uses(BLOCKS))
            for j in range(2):
                act.wait_ge(s_out[j], 32 * BLOCKS + 16)

        @block.vector
        def _(dve):
            dve.wait_ge(s_const, 64)
            nc.vector.memset(z[D:P], 0.0)

            def weight_lo(steps, u, base):
                if u >= len(steps):
                    return
                r = sum(step in streamed(steps) for step in steps[:u])
                src = raw_chunk(*steps[u], r)
                w = src.shape[1]
                dve.wait_ge(s_whi, base + u + 1)
                nc.vector.tensor_tensor(wlo[:, u % RING, 0:w], src, whi[:, u % RING, 0:w].bitcast(fp32),
                                        ALU.subtract).then_inc(s_wlo, 1)

            def odd_to_z(k, tiles):
                cols = slice(P * tiles.start, P * tiles.stop)
                return nc.vector.tensor_copy(z_of(2 * k + 1, tiles), by_sample(tgp[D:P, k % 2, cols]))

            def embedding_lo(n, k):
                dve.wait_ge(s_xhi, KT * n + k + 1)
                nc.vector.tensor_tensor(in_order(xlo[:, k % XRING, :]), by_sample(tgp[:, k % 2, 0:NB]),
                                        in_order(xhi[:, k % XRING, :].bitcast(fp32)), ALU.subtract)
                odd_to_z(k, tiles_left(n)).then_inc(s_xlo, 1)

            def gram_copies(n, jobs):
                for g in jobs:
                    dve.wait_ge(s_gram, GJ * n + g + 1)
                    for c in range(4):
                        last = nc.vector.tensor_copy(
                            dg[F * c:F * (c + 1), :, 4 * g:4 * g + 4].rearrange("p j q -> p q j"),
                            misc[F * c:F * (c + 1), g % 4, :].rearrange(
                                "p (q j) -> p q j", q=4)[:, :, F * c:F * (c + 1)])
                    last.then_inc(s_dgv, 1)

            def pairs_lo(n):
                dve.wait_ge(s_gchi, n + 1)
                nc.vector.tensor_tensor(gclo[:].rearrange("p t (c q) -> p c t q", c=4), gc[:],
                                        gchi[:].bitcast(fp32).rearrange("p t (c q) -> p c t q", c=4),
                                        ALU.subtract).then_inc(s_gclo, 1)

            def layer_lo(n, banks, src, hi, lo, bias, done, relued, hi_written, lo_written, per_block):
                dve.wait_ge(s_used, done)
                for j in banks:
                    for i in range(2):
                        last = nc.vector.tensor_scalar(src[:, j, NB * i:NB * (i + 1)],
                                                       src[:, j, NB * i:NB * (i + 1)],
                                                       bias[:, 2 * j + i:2 * j + i + 1], 0.0,
                                                       ALU.add, ALU.max)
                    last.then_inc(relued, 1)
                for j in banks:
                    dve.wait_ge(hi_written, per_block * n + j + 1)
                    nc.vector.tensor_tensor(lo[:, 2 * j:2 * j + 2, :],
                                            src[:, j, :].rearrange("p (i b) -> p i b", i=2),
                                            hi[:, 2 * j:2 * j + 2, :].bitcast(fp32),
                                            ALU.subtract).then_inc(lo_written, 1)

            def run(steps, after, n, m, base):
                if is_start(base):
                    for u in range(3):
                        weight_lo(steps, u, base)
                    for k in range(KT):
                        dve.wait_ge(s_zeven, k + 1)
                        odd_to_z(k, slice(0, 1)).then_inc(s_zodd, 1)
                    gram_copies(n, range(1, GJ // 2, 2))
                    embedding_lo(n, 0)
                    embedding_lo(n, 1)
                for u, (kind, k) in enumerate(steps):
                    for i, j in tiles_ahead(steps, after, u):
                        embedding_lo(n + i, j)
                    weight_lo(steps + after, u + 3, base)
                    if kind == "emb" and k == GRAM_AFTER - 1:
                        if is_start(base):
                            gram_copies(n, range(GJ // 2 + 1, GJ, 2))
                        else:
                            dve.wait_ge(s_gdw, 32 * n)
                            gram_copies(n, range(1, GJ, 2))
                    if kind == "l2" and k == 1:
                        layer_lo(m, [0], l2p, h2hi, h2lo, b2s, base + u + 1, s_h2r, s_h2hi, s_h2lo, 2)
                    if kind == "l2" and k == 3:
                        layer_lo(m, [1], l2p, h2hi, h2lo, b2s, base + u + 1, s_h2r, s_h2hi, s_h2lo, 2)
                    if (kind, k) in (("l2", 2), ("emb", KT - 1)) and n is not None and (
                            kind == "l2" or len(steps) == len(FIRST)):
                        pairs_lo(n)
                    if kind == "pair" and k == CROSS - 1:
                        layer_lo(n, range(4), h1p, h1hi, h1lo, b1s, base + u + 1, s_h1r, s_h1hi, s_h1lo, 4)

            run(FIRST, BODY, 0, None, 0)
            with dve.Fori(1, BLOCKS - 1) as n:
                run(BODY, BODY, n, n - 1, first_seq(n))
            n = BLOCKS - 1
            run(BODY, LAST, n, n - 1, first_seq(n))
            run(LAST, [], None, n, first_seq(BLOCKS))

        @block.tensor
        def _(pe):
            pe.wait_ge(s_const, 64)

            def three(dst, slot, cols, hi, lo, start, stop):
                nc.tensor.matmul(dst, whi[:, slot, cols], hi, start=start, stop=False, skip_group_check=True)
                nc.tensor.matmul(dst, whi[:, slot, cols], lo, start=False, stop=False, skip_group_check=True)
                return nc.tensor.matmul(dst, wlo[:, slot, cols], hi, start=False, stop=stop,
                                        skip_group_check=True)

            def early_transpose(k):
                pe.wait_ge(s_first[k], 32)
                if k >= 2:
                    pe.wait_ge(s_zodd, k - 1)
                nc.tensor.transpose(tgp[:, k % 2, 0:P], emb[:, k, 0, :], ident[:]).then_inc(s_early, 1)

            def transposes(n, k):
                pe.wait_ge(s_emb[k], 32 * BT * n + 32)
                if k >= 2:
                    pe.wait_ge(s_xlo, KT * n + k - 1)
                else:
                    before = GJ // 4 if isinstance(n, int) and n == 0 else GJ // 2 * n
                    pe.wait_ge(s_dga, before)
                    pe.wait_ge(s_dgv, before)
                for t in range(BT):
                    last = nc.tensor.transpose(tgp[:, k % 2, P * t:P * (t + 1)], emb[:, k, t, :], ident[:])
                last.then_inc(s_t, 1)

            def gram(n, jobs):
                for g in jobs:
                    if g >= 4:
                        pe.wait_ge(s_dgv if g % 2 else s_dga, GJ // 2 * n + g // 2 - 1)
                    for i in range(4):
                        zq = z[:, 4 * g + i, :, :].rearrange("d c f -> d (c f)")
                        last = nc.tensor.matmul(misc[:, g % 4, P * i:P * (i + 1)], zq, zq, start=True, stop=True)
                    last.then_inc(s_gram, 1)

            def run(steps, after, n, m, base):
                if is_start(base):
                    for k in range(KT):
                        early_transpose(k)
                    pe.wait_ge(s_zeven, KT)
                    pe.wait_ge(s_zodd, KT)
                    gram(n, range(GJ // 2))
                    transposes(n, 0)
                    transposes(n, 1)
                for u, (kind, k) in enumerate(steps):
                    if (kind, k) == ("emb", GRAM_AFTER):
                        pe.wait_ge(s_xhi, KT * n + KT)
                        pe.wait_ge(s_xlo, KT * n + KT)
                        if is_start(base):
                            gram(n, range(GJ // 2, GJ))
                        else:
                            gram(n, range(GJ))
                    for i, j in tiles_ahead(steps, after, u):
                        transposes(n + i, j)
                    pe.wait_ge(s_wlo, base + u + 1)
                    {"emb": layer1, "pair": layer1, "l2": layer2, "l3": layer3}[kind](
                        kind, k, u % RING, m if kind in ("l2", "l3") else n, base).then_inc(s_used, 1)

            def layer1(kind, k, slot, n, base):
                if kind == "emb":
                    pe.wait_ge(s_xlo, KT * n + k + 1)
                    hi, lo = xhi[:, k % XRING, :], xlo[:, k % XRING, :]
                else:
                    if k == 0:
                        pe.wait_ge(s_gclo, n + 1)
                    hi, lo = gchi[:, k, :], gclo[:, k, :]
                first, final = (kind, k) == EMB[0], (kind, k) == PAIR[-1]
                for j in range(H1 // P):
                    if first and not is_start(base) and j % 2 == 0:
                        pe.wait_ge(s_h1lo, 4 * (n - 1) + j // 2 + 1)
                    last = three(h1p[:, j // 2, NB * (j % 2):NB * (j % 2 + 1)], slot,
                                 slice(P * j, P * (j + 1)), hi, lo, first and j % 2 == 0, final)
                return last

            def layer2(kind, k, slot, m, base):
                bank, half = k // 2, k % 2
                grams = GJ // 2 * min(m + 2, BLOCKS) if isinstance(m, int) else GJ // 2 * (m + 2)
                if k == 0:
                    if isinstance(m, int):
                        pe.wait_ge(s_sig, 4 * m)
                    pe.wait_ge(s_dga, grams)
                    pe.wait_ge(s_dgv, grams)
                    pe.wait_ge(s_h1lo, 4 * m + 4)
                for c in range(4):
                    for i in range(2):
                        last = three(l2p[:, bank, NB * i:NB * (i + 1)], slot,
                                     slice(2 * P * c + P * i, 2 * P * c + P * (i + 1)),
                                     h1hi[:, 4 * half + c, :], h1lo[:, 4 * half + c, :],
                                     (half, c, i) == (0, 0, 0), (half, c) == (1, 3))
                return last

            def layer3(kind, k, slot, m, base):
                if k == 0:
                    pe.wait_ge(s_h2lo, 2 * m + 1)
                if k >= 2:
                    pe.wait_ge(s_sig, 4 * m + k - 1)
                for c in range(H2 // P):
                    if (k, c) == (0, 2):
                        pe.wait_ge(s_h2lo, 2 * m + 2)
                    for i in range(2):
                        last = three(l2p[0:OT, k % 2, NB * i:NB * (i + 1)], slot,
                                     slice(2 * OT * c + OT * i, 2 * OT * c + OT * (i + 1)),
                                     h2hi[:, c, :], h2lo[:, c, :], (c, i) == (0, 0), c == 3)
                return last

            run(FIRST, BODY, 0, None, 0)
            with pe.Fori(1, BLOCKS - 1) as n:
                run(BODY, BODY, n, n - 1, first_seq(n))
            n = BLOCKS - 1
            run(BODY, LAST, n, n - 1, first_seq(n))
            run(LAST, [], None, n, first_seq(BLOCKS))


def pair_rows():
    import numpy as np
    rows = np.full((CROSS, P), -1)
    for t in range(CROSS):
        for kk in range(4):
            shift = CROSS * kk + t + 1
            for i in range(F if shift < F // 2 else F // 2):
                a, b = sorted((i, (i + shift) % F))
                rows[t, F * kk + i] = F * D + a * F - a * (a + 1) // 2 + b - a - 1
    return rows


def kernel(r_x, L0_rec_emb_tables, L0_rec_W1, L0_rec_b1, L0_rec_W2, L0_rec_b2, L0_rec_W3, L0_rec_b3):
    import numpy as np
    import concourse.bacc as bacc
    from concourse import mybir as mb
    from concourse.bass_utils import run_bass_kernel_spmd

    w1_in = np.asarray(L0_rec_W1)
    rows = pair_rows()
    w_pair = np.zeros((CROSS * P, H1), w1_in.dtype)
    w_pair[rows.ravel() >= 0] = w1_in[rows[rows >= 0]]
    w1 = np.concatenate([w1_in[:F * D], w_pair]).reshape(KT + CROSS, P, H1)
    w2 = np.asarray(L0_rec_W2).reshape(2, 4, P, 2, 2 * P).transpose(3, 0, 2, 1, 4).reshape(4, P, 8 * P)
    w3 = np.asarray(L0_rec_W3).reshape(4, P, 4, 2 * OT).transpose(2, 1, 0, 3).reshape(4, P, 8 * OT)
    arrays = {
        "x": np.asarray(r_x).reshape(BLOCKS, 4, BT, P // 4, F).transpose(1, 3, 0, 2, 4).reshape(P, BLOCKS, BT, F),
        "tables": np.asarray(L0_rec_emb_tables).reshape(F * V, D),
        "w1": w1,
        "b1": np.asarray(L0_rec_b1).reshape(H1 // P, P).T,
        "w2": w2,
        "b2": np.asarray(L0_rec_b2).reshape(H2 // P, P).T,
        "w3": w3,
        "b3": np.asarray(L0_rec_b3).reshape(OUT // OT, OT).T,
        "ident": np.eye(P, dtype=np.float32),
    }
    nc = bacc.Bacc("TRN2", target_bir_lowering=False, num_devices=1)
    args = [nc.dram_tensor(k + "_dram", v.shape, mb.dt.from_np(v.dtype), kind="ExternalInput").ap()
            for k, v in arrays.items()]
    out = nc.dram_tensor("out_dram", (OUT, B), mb.dt.float32, kind="ExternalOutput").ap()
    recsys_kernel(nc, *args, out)
    r = run_bass_kernel_spmd(nc, [{k + "_dram": np.ascontiguousarray(v) for k, v in arrays.items()}], core_ids=[0])
    return np.ascontiguousarray(np.asarray(r.results[0]["out_dram"]).T)
```
